# Optimizing a Trainium2 kernel written in Bass

```python
import numpy as np
import jax
import jax.numpy as jnp

def _softmax(x, axis=-1):
    return jax.nn.softmax(x, axis=axis)

def _gelu(x):
    return jax.nn.gelu(x, approximate=True)

def _silu(x):
    return jax.nn.silu(x)

def _sigmoid(x):
    return jax.nn.sigmoid(x)

def _layernorm(x, axis=-1, eps=1e-05):
    m = jnp.mean(x, axis=axis, keepdims=True)
    v = jnp.var(x, axis=axis, keepdims=True)
    return (x - m) / jnp.sqrt(v + eps)

def _scatter_add(tgt, idx, src, axis=0):
    return tgt.at[idx].add(src)

def _segment_sum(src, seg, n):
    return jax.ops.segment_sum(src, seg, n)
kernel_name = 'mk_dlrm_tower_d1_rec_r8_7775a5'

def setup_inputs(seed: int=0):
    np.random.seed(seed)
    _w = jnp.asarray

    def _rec_inputs():
        import jax
        import jax.numpy as jnp
        _tk = jax.random.key(seed)
        ids = jnp.stack([jax.random.randint(jax.random.fold_in(_tk, 200 + f), (512,), 0, v, jnp.int32) for f, v in enumerate([125000, 12500, 12500, 12500, 1250, 1250, 1250, 1250, 1000, 12500, 1000, 1000, 1000, 1250, 12500, 1250, 1000, 1250, 1250, 12500, 12500, 12500, 1000, 1000, 1000, 1000])], axis=1)
        tbl_0 = 0.05 * jax.random.normal(jax.random.fold_in(_tk, 500 + 0), (125000, 128), jnp.float32)
        tbl_1 = 0.05 * jax.random.normal(jax.random.fold_in(_tk, 500 + 1), (12500, 128), jnp.float32)
        tbl_2 = 0.05 * jax.random.normal(jax.random.fold_in(_tk, 500 + 2), (12500, 128), jnp.float32)
        tbl_3 = 0.05 * jax.random.normal(jax.random.fold_in(_tk, 500 + 3), (12500, 128), jnp.float32)
        tbl_4 = 0.05 * jax.random.normal(jax.random.fold_in(_tk, 500 + 4), (1250, 128), jnp.float32)
        tbl_5 = 0.05 * jax.random.normal(jax.random.fold_in(_tk, 500 + 5), (1250, 128), jnp.float32)
        tbl_6 = 0.05 * jax.random.normal(jax.random.fold_in(_tk, 500 + 6), (1250, 128), jnp.float32)
        tbl_7 = 0.05 * jax.random.normal(jax.random.fold_in(_tk, 500 + 7), (1250, 128), jnp.float32)
        tbl_8 = 0.05 * jax.random.normal(jax.random.fold_in(_tk, 500 + 8), (1000, 128), jnp.float32)
        tbl_9 = 0.05 * jax.random.normal(jax.random.fold_in(_tk, 500 + 9), (12500, 128), jnp.float32)
        tbl_10 = 0.05 * jax.random.normal(jax.random.fold_in(_tk, 500 + 10), (1000, 128), jnp.float32)
        tbl_11 = 0.05 * jax.random.normal(jax.random.fold_in(_tk, 500 + 11), (1000, 128), jnp.float32)
        tbl_12 = 0.05 * jax.random.normal(jax.random.fold_in(_tk, 500 + 12), (1000, 128), jnp.float32)
        tbl_13 = 0.05 * jax.random.normal(jax.random.fold_in(_tk, 500 + 13), (1250, 128), jnp.float32)
        tbl_14 = 0.05 * jax.random.normal(jax.random.fold_in(_tk, 500 + 14), (12500, 128), jnp.float32)
        tbl_15 = 0.05 * jax.random.normal(jax.random.fold_in(_tk, 500 + 15), (1250, 128), jnp.float32)
        tbl_16 = 0.05 * jax.random.normal(jax.random.fold_in(_tk, 500 + 16), (1000, 128), jnp.float32)
        tbl_17 = 0.05 * jax.random.normal(jax.random.fold_in(_tk, 500 + 17), (1250, 128), jnp.float32)
        tbl_18 = 0.05 * jax.random.normal(jax.random.fold_in(_tk, 500 + 18), (1250, 128), jnp.float32)
        tbl_19 = 0.05 * jax.random.normal(jax.random.fold_in(_tk, 500 + 19), (12500, 128), jnp.float32)
        tbl_20 = 0.05 * jax.random.normal(jax.random.fold_in(_tk, 500 + 20), (12500, 128), jnp.float32)
        tbl_21 = 0.05 * jax.random.normal(jax.random.fold_in(_tk, 500 + 21), (12500, 128), jnp.float32)
        tbl_22 = 0.05 * jax.random.normal(jax.random.fold_in(_tk, 500 + 22), (1000, 128), jnp.float32)
        tbl_23 = 0.05 * jax.random.normal(jax.random.fold_in(_tk, 500 + 23), (1000, 128), jnp.float32)
        tbl_24 = 0.05 * jax.random.normal(jax.random.fold_in(_tk, 500 + 24), (1000, 128), jnp.float32)
        tbl_25 = 0.05 * jax.random.normal(jax.random.fold_in(_tk, 500 + 25), (1000, 128), jnp.float32)
        _rk = jax.random.fold_in(_tk, 7)
        r_dense_features = -0.000520686 + 1.00062 * jax.random.normal(jax.random.fold_in(_rk, 101), (512, 128), jnp.float32)
        W_top1 = 0.0405887 * jax.random.normal(jax.random.fold_in(_tk, 801), (607, 512), jnp.float32)
        W_top2 = 0.0441942 * jax.random.normal(jax.random.fold_in(_tk, 802), (512, 256), jnp.float32)
        W_top3 = 0.0625 * jax.random.normal(jax.random.fold_in(_tk, 803), (256, 1), jnp.float32)
        b_top1 = jnp.zeros((512,), jnp.float32)
        b_top2 = jnp.zeros((256,), jnp.float32)
        return (r_dense_features, ids, tbl_0, tbl_1, tbl_2, tbl_3, tbl_4, tbl_5, tbl_6, tbl_7, tbl_8, tbl_9, tbl_10, tbl_11, tbl_12, tbl_13, tbl_14, tbl_15, tbl_16, tbl_17, tbl_18, tbl_19, tbl_20, tbl_21, tbl_22, tbl_23, tbl_24, tbl_25, W_top1, b_top1, W_top2, b_top2, W_top3)
    r_dense_features, ids, tbl_0, tbl_1, tbl_2, tbl_3, tbl_4, tbl_5, tbl_6, tbl_7, tbl_8, tbl_9, tbl_10, tbl_11, tbl_12, tbl_13, tbl_14, tbl_15, tbl_16, tbl_17, tbl_18, tbl_19, tbl_20, tbl_21, tbl_22, tbl_23, tbl_24, tbl_25, W_top1, b_top1, W_top2, b_top2, W_top3 = _rec_inputs()

    def _L0_rec_setup():
        import jax, jax.numpy as jnp
        import numpy as np
        F = 26
        key = jax.random.key(seed)
        k1, k2 = jax.random.split(key)
        B, D = (2048, 128)
        dense_features = jax.random.normal(k1, (B, D), dtype=jnp.float32)
        sparse_features = jax.random.normal(k2, (B, F, D), dtype=jnp.float32)
        return {'dense_features': dense_features, 'sparse_features': sparse_features}
    _L0_rec_all = _L0_rec_setup()
    _L0_rec_in = {k: v for k, v in _L0_rec_all.items() if k in ()}
    del _L0_rec_all
    return {'r_dense_features': r_dense_features, 'ids': ids, 'tbl_0': tbl_0, 'tbl_1': tbl_1, 'tbl_2': tbl_2, 'tbl_3': tbl_3, 'tbl_4': tbl_4, 'tbl_5': tbl_5, 'tbl_6': tbl_6, 'tbl_7': tbl_7, 'tbl_8': tbl_8, 'tbl_9': tbl_9, 'tbl_10': tbl_10, 'tbl_11': tbl_11, 'tbl_12': tbl_12, 'tbl_13': tbl_13, 'tbl_14': tbl_14, 'tbl_15': tbl_15, 'tbl_16': tbl_16, 'tbl_17': tbl_17, 'tbl_18': tbl_18, 'tbl_19': tbl_19, 'tbl_20': tbl_20, 'tbl_21': tbl_21, 'tbl_22': tbl_22, 'tbl_23': tbl_23, 'tbl_24': tbl_24, 'tbl_25': tbl_25, 'W_top1': W_top1, 'b_top1': b_top1, 'W_top2': W_top2, 'b_top2': b_top2, 'W_top3': W_top3}

def reference(r_dense_features, ids, tbl_0, tbl_1, tbl_2, tbl_3, tbl_4, tbl_5, tbl_6, tbl_7, tbl_8, tbl_9, tbl_10, tbl_11, tbl_12, tbl_13, tbl_14, tbl_15, tbl_16, tbl_17, tbl_18, tbl_19, tbl_20, tbl_21, tbl_22, tbl_23, tbl_24, tbl_25, W_top1, b_top1, W_top2, b_top2, W_top3):
    import jax
    import jax.numpy as jnp

    def _L0_rec_ref(dense_features, sparse_features):
        import jax, jax.numpy as jnp
        import numpy as np
        F = 26
        B, D = dense_features.shape
        combined = jnp.concatenate((dense_features[:, None, :], sparse_features), axis=1)
        interactions = jnp.einsum('bfd,bgd->bfg', combined, combined)
        iu, ju = jnp.triu_indices(F + 1, k=1)
        interactions_flat = interactions[:, iu, ju]
        return jnp.concatenate((dense_features, interactions_flat), axis=1)
    e = jnp.stack([tbl_0[ids[:, 0]], tbl_1[ids[:, 1]], tbl_2[ids[:, 2]], tbl_3[ids[:, 3]], tbl_4[ids[:, 4]], tbl_5[ids[:, 5]], tbl_6[ids[:, 6]], tbl_7[ids[:, 7]], tbl_8[ids[:, 8]], tbl_9[ids[:, 9]], tbl_10[ids[:, 10]], tbl_11[ids[:, 11]], tbl_12[ids[:, 12]], tbl_13[ids[:, 13]], tbl_14[ids[:, 14]], tbl_15[ids[:, 15]], tbl_16[ids[:, 16]], tbl_17[ids[:, 17]], tbl_18[ids[:, 18]], tbl_19[ids[:, 19]], tbl_20[ids[:, 20]], tbl_21[ids[:, 21]], tbl_22[ids[:, 22]], tbl_23[ids[:, 23]], tbl_24[ids[:, 24]], tbl_25[ids[:, 25]]], axis=1)
    z = _L0_rec_ref(r_dense_features, e)
    z = z.reshape(z.shape[0], -1)
    h = jnp.concatenate([z, r_dense_features], axis=1)
    h = jnp.maximum(h @ W_top1 + b_top1, 0.0)
    h = jnp.maximum(h @ W_top2 + b_top2, 0.0)
    y = h @ W_top3
    return y

_drawn_inputs = setup_inputs


def setup_inputs(seed=0):
    import zlib

    import numpy as np

    out = dict(_drawn_inputs(seed))
    spreads = {'b_top1': (0.0, 0.1), 'b_top2': (0.0, 0.1)}
    factors = {}
    for name, (base, spread) in spreads.items():
        noise = np.random.default_rng([zlib.crc32(name.encode()), seed]).standard_normal(out[name].shape)
        drawn = base * np.exp(spread * noise) if base else spread * noise
        out[name] = jnp.asarray(drawn.astype(out[name].dtype))
    for name, factor in factors.items():
        out[name] = (out[name] * factor).astype(out[name].dtype)
    return out
```

```python
import concourse.bass as bass
from concourse import mybir
from contextlib import ExitStack

BATCH = 512
DIM = 128
TABLES = 26
FEATS = TABLES + 1
ROWS = 128
TILES = BATCH // ROWS
HID1, HID2 = 512, 256
PAIRS = FEATS * (FEATS - 1) // 2

FEATS_PER_GROUP = 4
GROUPS = [range(f, min(f + FEATS_PER_GROUP, FEATS)) for f in range(0, FEATS, FEATS_PER_GROUP)]
GROUPS_OF_BANK = [len(GROUPS[b::2]) for b in range(2)]

PAIR_ROWS = FEATS - 1
BUNCH = 16
BUNCHES = ROWS // BUNCH
BUNCHES_OF_BANK = BUNCHES // 2

QUADS, QUAD = 4, 32
CHUNKS = -(-PAIR_ROWS // QUADS)
H1_TILES = HID1 // 128
H2_TILES = HID2 // 128


def dlrm_tower(nc, dense, ids, tables, w_dense, w_pairs, b1, w2, b2, w3, out):
    fp32 = mybir.dt.float32
    i32 = mybir.dt.int32
    ALU = mybir.AluOpType
    ACT = mybir.ActivationFunctionType

    ctx = ExitStack()
    with ctx:
        def sb(name, shape, dt=fp32):
            return ctx.enter_context(nc.sbuf_tensor(name, shape, dt))

        def bank(name):
            return ctx.enter_context(nc.psum_tensor(name, [128, 512], fp32))

        def sem(name):
            return ctx.enter_context(nc.semaphore(name))

        idx = sb("idx", [ROWS, TILES, TABLES], i32)
        emb = sb("emb", [ROWS, FEATS, DIM])
        embT = sb("embT", [DIM, ROWS, FEATS])
        z = sb("z", [128, CHUNKS, ROWS])
        h1 = sb("h1", [128, H1_TILES, ROWS])
        h2 = sb("h2", [128, H2_TILES, ROWS])
        y = sb("y", [1, BATCH])
        wd_sb = sb("wd_sb", [DIM, 2, HID1])
        wp_sb = sb("wp_sb", [128, CHUNKS, HID1])
        w2_sb = sb("w2_sb", [128, H1_TILES, HID2])
        w3_sb = sb("w3_sb", [128, H2_TILES])
        b1_sb = sb("b1_sb", [128, H1_TILES])
        b2_sb = sb("b2_sb", [128, H2_TILES])
        ident = sb("ident", [128, 128])
        start_mark = sb("start_mark", [1, 4])

        ps_t = [bank(f"ps_t{b}") for b in range(2)]
        ps_g = [bank(f"ps_g{b}") for b in range(2)]
        ps_h1 = [bank(f"ps_h1{b}") for b in range(2)]
        ps_h2 = [bank(f"ps_h2{m}") for m in range(H2_TILES)]
        ps_y = ps_h2[0][0:1, ROWS:2 * ROWS]

        idx0_in = sem("idx0_in")
        idx_in = sem("idx_in")
        dense_in = sem("dense_in")
        gathered = [sem(f"gathered{g}") for g in range(len(GROUPS))]
        wd_in = sem("wd_in")
        wp_in = sem("wp_in")
        w2_in = sem("w2_in")
        small_in = sem("small_in")
        ident_clear = sem("ident_clear")
        ident_ready = sem("ident_ready")
        z_clear = sem("z_clear")
        transposed = sem("transposed")
        t_free = [sem(f"t_free{b}") for b in range(2)]
        products = sem("products")
        g_free = [sem(f"g_free{b}") for b in range(2)]
        h1_sum = sem("h1_sum")
        h1_ready = [sem(f"h1_ready{b}") for b in range(2)]
        h2_sum = sem("h2_sum")
        h2_ready = sem("h2_ready")
        y_sum = sem("y_sum")
        y_ready = sem("y_ready")
        out_done = sem("out_done")

        block = ctx.enter_context(nc.Block())

        def copy_transposes(eng, copy, t, b):
            for n, feats in enumerate(GROUPS[b::2]):
                eng.wait_ge(transposed, t * len(GROUPS) + 2 * n + b + 1)
                k = len(feats)
                src = ps_t[b][:, 0:k * ROWS].rearrange("p (f s) -> p s f", f=k)
                copy(embT[:, :, feats[0]:feats[0] + k], src).then_inc(t_free[b], 1)

        def copy_products(eng, copy, t, b):
            for n in range(BUNCHES_OF_BANK):
                i = 2 * n + b
                eng.wait_ge(products, t * BUNCHES + i + 1)
                src = ps_g[b][0:PAIR_ROWS, 0:BUNCH * PAIR_ROWS].rearrange("p (s g) -> p g s", g=PAIR_ROWS)
                for j in range(QUADS):
                    cols = src[:, j::QUADS, :]
                    last = copy(z[QUAD * j:QUAD * j + PAIR_ROWS, 0:cols.shape[1], i * BUNCH:(i + 1) * BUNCH], cols)
                last.then_inc(g_free[b], 1)

        @block.sync
        def _(sp):
            ids_v = ids.rearrange("(t p) f -> p t f", p=ROWS)
            sp.dma_start(idx[:, 0, :], ids_v[:, 0, :]).then_inc(idx0_in, 16)
            sp.dma_start(emb[:, 0, :], dense[0:ROWS, :]).then_inc(dense_in, 16)
            sp.dma_start(idx[:, 1:TILES, :], ids_v[:, 1:TILES, :]).then_inc(idx_in, 16)
            sp.dma_start(wd_sb[:, :, :], w_dense).then_inc(wd_in, 16)
            sp.dma_start(wp_sb[:, :, :], w_pairs).then_inc(wp_in, 16)
            sp.dma_start(w2_sb[:, :, :], w2.rearrange("(k p) n -> p k n", p=128)).then_inc(w2_in, 16)
            sp.dma_start(w3_sb[:, :], w3).then_inc(small_in, 16)
            sp.dma_start(b1_sb[:, :], b1).then_inc(small_in, 16)
            sp.dma_start(b2_sb[:, :], b2).then_inc(small_in, 16)
            with sp.Fori(1, TILES) as t:
                sp.wait_ge(transposed, (t - 1) * len(GROUPS) + 1)
                sp.dma_start(emb[:, 0, :], dense[bass.ds(t * ROWS, ROWS), :]).then_inc(dense_in, 16)
            sp.wait_ge(y_ready, TILES)
            sp.dma_start(out.rearrange("b o -> o b"), y[:, :]).then_inc(out_done, 16)
            sp.wait_ge(out_done, 16)

        @block.gpsimd
        def _(pool):
            nc.gpsimd.memset(ident[:, :], 0.0).then_inc(ident_clear, 1)
            pool.wait_ge(ident_clear, 1)
            nc.gpsimd.affine_select(out=ident[:, :], in_=ident[:, :], compare_op=ALU.not_equal, fill=1.0,
                                    base=0, pattern=[[-1, 128]], channel_multiplier=1).then_inc(ident_ready, 1)
            pool.wait_ge(idx0_in, 16)

            def gather(t, f, g):
                pool.indirect_dma_start(emb[:, f, :], None, tables[f - 1],
                                        bass.IndirectOffsetOnAxis(idx[:, t, f - 1:f], 0)).then_inc(gathered[g], 16)

            for g, feats in enumerate(GROUPS):
                for f in feats:
                    if f:
                        gather(0, f, g)
            pool.wait_ge(idx_in, 16)
            for t in range(1, TILES):
                for g, feats in enumerate(GROUPS):
                    pool.wait_ge(transposed, (t - 1) * len(GROUPS) + g + 1)
                    for f in feats:
                        if f:
                            gather(t, f, g)

        @block.tensor
        def _(pe):
            pe.wait_ge(ident_ready, 1)
            pe.wait_ge(wd_in, 16)
            pe.wait_ge(wp_in, 16)
            pe.wait_ge(w2_in, 16)
            pe.wait_ge(small_in, 48)
            with pe.Fori(0, TILES) as t:
                for g, feats in enumerate(GROUPS):
                    rows = len([f for f in feats if f])
                    if g == 0:
                        pe.wait_ge(dense_in, (t + 1) * 16)
                    pe.wait_ge(gathered[g], (t + 1) * (16 * rows))
                    pe.wait_ge(t_free[g % 2], t * GROUPS_OF_BANK[g % 2] + g // 2 + 1)
                    for k, f in enumerate(feats):
                        last = nc.tensor.transpose(ps_t[g % 2][:, k * ROWS:(k + 1) * ROWS], emb[:, f, :], ident[:, :])
                    last.then_inc(transposed, 1)

                for b in range(2):
                    pe.wait_ge(t_free[b], (t + 1) * GROUPS_OF_BANK[b] + 1)
                for i in range(BUNCHES):
                    pe.wait_ge(g_free[i % 2], t * BUNCHES_OF_BANK + i // 2 + 1)
                    for s in range(BUNCH):
                        row = i * BUNCH + s
                        last = nc.tensor.matmul(ps_g[i % 2][0:PAIR_ROWS, s * PAIR_ROWS:(s + 1) * PAIR_ROWS],
                                                embT[:, row, 0:PAIR_ROWS], embT[:, row, 1:FEATS],
                                                start=True, stop=True)
                    last.then_inc(products, 1)

                def h1_out(n):
                    return ps_h1[n // 2][:, (n % 2) * ROWS:(n % 2 + 1) * ROWS]

                for n in range(H1_TILES):
                    for c in range(2):
                        nc.tensor.matmul(h1_out(n), wd_sb[:, c, n * 128:(n + 1) * 128], embT[:, :, 0],
                                         start=(c == 0 and n % 2 == 0), stop=False, skip_group_check=True)
                for b in range(2):
                    pe.wait_ge(g_free[b], (t + 1) * BUNCHES_OF_BANK + 1)
                for n in range(H1_TILES):
                    for q in range(CHUNKS):
                        last = nc.tensor.matmul(h1_out(n), wp_sb[:, q, n * 128:(n + 1) * 128], z[:, q, :],
                                                start=False, stop=(q == CHUNKS - 1), skip_group_check=True)
                    if n % 2:
                        last.then_inc(h1_sum, 1)

                for b in range(2):
                    pe.wait_ge(h1_ready[b], t + 1)
                for m in range(H2_TILES):
                    for k in range(H1_TILES):
                        last = nc.tensor.matmul(ps_h2[m][:, 0:ROWS], w2_sb[:, k, m * 128:(m + 1) * 128], h1[:, k, :],
                                                start=(k == 0), stop=(k == H1_TILES - 1))
                    last.then_inc(h2_sum, 1)

                pe.wait_ge(h2_ready, (t + 1) * H2_TILES)
                for k in range(H2_TILES):
                    last = nc.tensor.matmul(ps_y, w3_sb[:, k:k + 1], h2[:, k, :],
                                            start=(k == 0), stop=(k == H2_TILES - 1))
                last.then_inc(y_sum, 1)

        @block.vector
        def _(dve):
            nc.vector.memset(z[:, :, :], 0.0).then_inc(z_clear, 1)
            nc.vector.memset(start_mark[:, 0:1], 0.0).then_inc(t_free[0], 1)
            nc.vector.memset(start_mark[:, 1:2], 0.0).then_inc(t_free[1], 1)
            nc.vector.memset(start_mark[:, 2:3], 0.0).then_inc(g_free[0], 1)
            nc.vector.memset(start_mark[:, 3:4], 0.0).then_inc(g_free[1], 1)
            dve.wait_ge(z_clear, 1)
            dve.wait_ge(small_in, 48)
            with dve.Fori(0, TILES) as t:
                copy_transposes(dve, nc.vector.tensor_copy, t, 0)
                copy_products(dve, nc.vector.tensor_copy, t, 0)
                dve.wait_ge(h1_sum, t * 2 + 1)
                for n in (0, 1):
                    last = nc.vector.tensor_scalar(h1[:, n, :], ps_h1[0][:, n * ROWS:(n + 1) * ROWS],
                                                   b1_sb[:, n:n + 1], 0.0, ALU.add, ALU.max)
                last.then_inc(h1_ready[0], 1)
                dve.wait_ge(h2_sum, t * H2_TILES + 1)
                nc.vector.tensor_scalar(h2[:, 0, :], ps_h2[0][:, 0:ROWS], b2_sb[:, 0:1], 0.0,
                                        ALU.add, ALU.max).then_inc(h2_ready, 1)
                dve.wait_ge(y_sum, t + 1)
                nc.vector.tensor_copy(y[:, bass.ds(t * ROWS, ROWS)], ps_y).then_inc(y_ready, 1)

        @block.scalar
        def _(act):
            act.wait_ge(z_clear, 1)
            act.wait_ge(small_in, 48)
            with act.Fori(0, TILES) as t:
                copy_transposes(act, nc.scalar.copy, t, 1)
                copy_products(act, nc.scalar.copy, t, 1)
                act.wait_ge(h1_sum, t * 2 + 2)
                for n in (2, 3):
                    last = nc.scalar.activation(h1[:, n, :], ps_h1[1][:, (n - 2) * ROWS:(n - 1) * ROWS],
                                                ACT.Relu, bias=b1_sb[:, n:n + 1])
                last.then_inc(h1_ready[1], 1)
                act.wait_ge(h2_sum, t * H2_TILES + 2)
                nc.scalar.activation(h2[:, 1, :], ps_h2[1][:, 0:ROWS], ACT.Relu,
                                     bias=b2_sb[:, 1:2]).then_inc(h2_ready, 1)


def lay_out(inputs):
    import numpy as np
    arrays = {"dense": inputs["r_dense_features"], "ids": inputs["ids"]}
    for i in range(TABLES):
        arrays[f"tbl_{i}"] = inputs[f"tbl_{i}"]
    w1 = np.asarray(inputs["W_top1"])
    arrays["w_dense"] = np.stack([w1[:DIM], w1[DIM + PAIRS:]], axis=1)
    w_pairs = np.zeros((128, CHUNKS, HID1), w1.dtype)
    row = DIM
    for f in range(FEATS):
        for g in range(f + 1, FEATS):
            q, j = divmod(g - 1, QUADS)
            w_pairs[QUAD * j + f, q] = w1[row]
            row += 1
    arrays["w_pairs"] = w_pairs
    arrays["b1"] = np.asarray(inputs["b_top1"]).reshape(H1_TILES, 128).T
    arrays["w2"] = inputs["W_top2"]
    arrays["b2"] = np.asarray(inputs["b_top2"]).reshape(H2_TILES, 128).T
    arrays["w3"] = np.asarray(inputs["W_top3"]).reshape(H2_TILES, 128).T
    return {name: np.ascontiguousarray(a) for name, a in arrays.items()}


def kernel(**inputs):
    import concourse.bacc as _bacc
    from concourse import mybir as _mybir
    from concourse.bass_utils import run_bass_kernel_spmd as _run

    nc = _bacc.Bacc("TRN2", target_bir_lowering=False, num_devices=1)
    arrays = lay_out(inputs)
    ap = {name: nc.dram_tensor(f"in_{name}", a.shape, _mybir.dt.from_np(a.dtype), kind="ExternalInput").ap()
          for name, a in arrays.items()}
    out = nc.dram_tensor("out_y", (BATCH, 1), _mybir.dt.float32, kind="ExternalOutput").ap()
    dlrm_tower(nc, ap["dense"], ap["ids"], [ap[f"tbl_{i}"] for i in range(TABLES)], ap["w_dense"], ap["w_pairs"],
               ap["b1"], ap["w2"], ap["b2"], ap["w3"], out)
    r = _run(nc, [{f"in_{name}": a for name, a in arrays.items()}], core_ids=[0])
    return r.results[0]["out_y"]
```

```python
import concourse.bass as bass
from concourse import mybir
from contextlib import ExitStack

BATCH = 512
DIM = 128
TABLES = 26
FEATS = TABLES + 1
ROWS = 128
TILES = BATCH // ROWS
HID1, HID2 = 512, 256
PAIRS = FEATS * (FEATS - 1) // 2

PICKED = [8, 10, 11, 12]
PICKS = len(PICKED)
PICK_VOCAB = 1000
PICK_CHUNKS = 8
PICK_PARTS = PICK_VOCAB // PICK_CHUNKS
PIECES = 3

GATHERED = [i for i in range(TABLES) if i not in PICKED]
FIXED = 1 + PICKS
SLOTS = [0] + [i + 1 for i in PICKED] + [i + 1 for i in GATHERED]

RING = 4
GROUP_SIZES = [4, 4, 4, 4, 2, 2, 1, 1]
GROUPS = [range(sum(GROUP_SIZES[:g]), sum(GROUP_SIZES[:g + 1])) for g in range(len(GROUP_SIZES))]
PAIR_ROWS = FEATS - 1
BUNCH = 16
BUNCHES = ROWS // BUNCH
USES = len(GROUPS) + BUNCHES
assert sum(GROUP_SIZES) == len(GATHERED) and USES % RING == 0 and len(GROUPS) % RING == 0

GROUPS_AFTER_PICK = [(0, 1), (2,), (3,), (4, 5, 6, 7)]

QUADS, QUAD = 4, 32
CHUNKS = -(-PAIR_ROWS // QUADS)
H1_TILES = HID1 // 128
H2_TILES = HID2 // 128


def dlrm_tower(nc, dense, ids, ids_picked, tables, w_dense, w_pairs, b1, w2, b2, w3, out):
    fp32 = mybir.dt.float32
    bf16 = mybir.dt.bfloat16
    i32 = mybir.dt.int32
    i16 = mybir.dt.int16
    ALU = mybir.AluOpType
    ACT = mybir.ActivationFunctionType

    ctx = ExitStack()
    with ctx:
        def sb(name, shape, dt=fp32):
            return ctx.enter_context(nc.sbuf_tensor(name, shape, dt))

        def bank(name):
            return ctx.enter_context(nc.psum_tensor(name, [128, 512], fp32))

        def sem(name):
            return ctx.enter_context(nc.semaphore(name))

        idx = sb("idx", [ROWS, TILES, TABLES], i32)
        emb = sb("emb", [ROWS, len(GATHERED), DIM])
        dense_sb = sb("dense_sb", [ROWS, TILES, DIM])
        fixedT = sb("fixedT", [DIM, FIXED, BATCH])
        embT = sb("embT", [DIM, ROWS, FEATS])
        pick_ids32 = sb("pick_ids32", [PICK_PARTS, PICKS, BATCH], i32)
        pick_ids = sb("pick_ids", [PICK_PARTS, PICKS, BATCH], i16)
        vocab = sb("vocab", [PICK_PARTS, PICK_CHUNKS])
        one_hot = [sb(f"one_hot{b}", [PICK_PARTS, PICK_CHUNKS, BATCH], bf16) for b in range(2)]
        table = sb("table", [PICK_PARTS, PICKS, PICK_CHUNKS * DIM])
        rest = sb("rest", [PICK_PARTS, PICKS, PICK_CHUNKS * DIM])
        piece = [sb(f"piece{n}", [PICK_PARTS, PICKS, PICK_CHUNKS * DIM], bf16) for n in range(PIECES)]
        z = sb("z", [128, CHUNKS, ROWS])
        h1 = sb("h1", [128, H1_TILES, ROWS])
        h2 = sb("h2", [128, H2_TILES, ROWS])
        y = sb("y", [1, BATCH])
        wd_in2 = sb("wd_in2", [DIM, 2, HID1])
        wd_sb = sb("wd_sb", [DIM, HID1])
        wp_sb = sb("wp_sb", [128, CHUNKS, HID1])
        w2_sb = sb("w2_sb", [128, H1_TILES, HID2])
        w3_sb = sb("w3_sb", [128, H2_TILES])
        b1_sb = sb("b1_sb", [128, H1_TILES])
        b2_sb = sb("b2_sb", [128, H2_TILES])
        ident = sb("ident", [128, 128])

        ring = [bank(f"ring{b}") for b in range(RING)]
        ps_h1 = [bank(f"ps_h1{b}") for b in range(2)]
        ps_h2 = [bank(f"ps_h2{m}") for m in range(H2_TILES)]
        ps_y = ps_h2[0][0:1, ROWS:2 * ROWS]
        ps_pick = ps_h2
        ps_dense = ps_h1[0]

        idx0_in = sem("idx0_in")
        idx_in = sem("idx_in")
        dense_in = sem("dense_in")
        pick_ids_in = [sem(f"pick_ids_in{i}") for i in range(PICKS)]
        table_in = [sem(f"table_in{i}") for i in range(PICKS)]
        gathered = [sem(f"gathered{g}") for g in range(len(GROUPS))]
        wd_in = sem("wd_in")
        wp_in = sem("wp_in")
        w2_in = sem("w2_in")
        small_in = sem("small_in")
        ident_clear = sem("ident_clear")
        ident_ready = sem("ident_ready")
        vocab_ready = sem("vocab_ready")
        z_clear = sem("z_clear")
        wd_ready = sem("wd_ready")
        pick_ids_ready = sem("pick_ids_ready")
        piece_ready = [sem(f"piece_ready{n}") for n in range(PIECES)]
        rest_ready = sem("rest_ready")
        one_hot_ready = sem("one_hot_ready")
        picked = sem("picked")
        dense_turned = sem("dense_turned")
        pick_out = sem("pick_out")
        dense_out = sem("dense_out")
        fixed_placed = sem("fixed_placed")
        filled = sem("filled")
        emptied = [sem(f"emptied{b}") for b in range(RING)]
        h1_sum = sem("h1_sum")
        h1_ready = [sem(f"h1_ready{b}") for b in range(2)]
        h2_sum = sem("h2_sum")
        h2_ready = sem("h2_ready")
        y_sum = sem("y_sum")
        y_ready = sem("y_ready")
        out_done = sem("out_done")

        block = ctx.enter_context(nc.Block())

        def group_use(t, g):
            return t * USES + g

        def bunch_use(t, i):
            return t * USES + len(GROUPS) + i

        def copy_group(eng, copy, t, g):
            eng.wait_ge(filled, group_use(t, g) + 1)
            k = len(GROUPS[g])
            src = ring[g % RING][:, 0:k * ROWS].rearrange("p (f s) -> p s f", f=k)
            first = FIXED + GROUPS[g][0]
            copy(embT[:, :, first:first + k], src).then_inc(emptied[g % RING], 1)

        def copy_bunch(eng, copy, t, i):
            eng.wait_ge(filled, bunch_use(t, i) + 1)
            src = ring[i % RING][0:PAIR_ROWS, 0:BUNCH * PAIR_ROWS].rearrange("p (s g) -> p g s", g=PAIR_ROWS)
            for j in range(QUADS):
                cols = src[:, j::QUADS, :]
                last = copy(z[QUAD * j:QUAD * j + PAIR_ROWS, 0:cols.shape[1], i * BUNCH:(i + 1) * BUNCH], cols)
            last.then_inc(emptied[i % RING], 1)

        @block.sync
        def _(sp):
            ids_v = ids.rearrange("(t p) f -> p t f", p=ROWS)
            sp.dma_start(idx[:, 0, :], ids_v[:, 0, :]).then_inc(idx0_in, 16)
            for i in range(PICKS):
                sp.dma_start(pick_ids32[:, i, :], ids_picked[i:i + 1, :].to_broadcast([PICK_PARTS, BATCH])
                             ).then_inc(pick_ids_in[i], 16)
                if i == 0:
                    sp.dma_start(dense_sb[:, :, :], dense.rearrange("(t p) d -> p t d", p=ROWS)
                                 ).then_inc(dense_in, 16)
                else:
                    sp.dma_start(table[:, i, :], tables[PICKED[i]].rearrange("(p c) d -> p (c d)", c=PICK_CHUNKS)
                                 ).then_inc(table_in[i], 16)
            sp.dma_start(idx[:, 1:TILES, :], ids_v[:, 1:TILES, :]).then_inc(idx_in, 16)
            sp.dma_start(wd_in2[:, :, :], w_dense).then_inc(wd_in, 16)
            sp.dma_start(wp_sb[:, :, :], w_pairs).then_inc(wp_in, 16)
            sp.dma_start(w2_sb[:, :, :], w2.rearrange("(k p) n -> p k n", p=128)).then_inc(w2_in, 16)
            sp.dma_start(w3_sb[:, :], w3).then_inc(small_in, 16)
            sp.dma_start(b1_sb[:, :], b1).then_inc(small_in, 16)
            sp.dma_start(b2_sb[:, :], b2).then_inc(small_in, 16)
            sp.wait_ge(y_ready, TILES)
            sp.dma_start(out.rearrange("b o -> o b"), y[:, :]).then_inc(out_done, 16)
            sp.wait_ge(out_done, 16)

        @block.gpsimd
        def _(pool):
            nc.gpsimd.memset(ident[:, :], 0.0).then_inc(ident_clear, 1)
            nc.gpsimd.iota(vocab[:, :], [[1, PICK_CHUNKS]], base=0, channel_multiplier=PICK_CHUNKS,
                           allow_small_or_imprecise_dtypes=True).then_inc(vocab_ready, 1)
            pool.wait_ge(ident_clear, 1)
            nc.gpsimd.affine_select(out=ident[:, :], in_=ident[:, :], compare_op=ALU.not_equal, fill=1.0,
                                    base=0, pattern=[[-1, 128]], channel_multiplier=1).then_inc(ident_ready, 1)
            pool.wait_ge(idx0_in, 16)
            for t in range(TILES):
                if t == 1:
                    pool.wait_ge(idx_in, 16)
                for g, feats in enumerate(GROUPS):
                    if t:
                        pool.wait_ge(filled, group_use(t - 1, g) + 1)
                    for k in feats:
                        i = GATHERED[k]
                        pool.indirect_dma_start(emb[:, k, :], None, tables[i],
                                                bass.IndirectOffsetOnAxis(idx[:, t, i:i + 1], 0)
                                                ).then_inc(gathered[g], 16)

        @block.tensor
        def _(pe):
            def transpose_group(t, g):
                if not (isinstance(t, int) and t == 0):
                    pe.wait_ge(gathered[g], (t + 1) * (16 * len(GROUPS[g])))
                    pe.wait_ge(emptied[g % RING], t * (USES // RING) + g // RING)
                else:
                    pe.wait_ge(gathered[g], 16 * len(GROUPS[g]))
                    if g >= RING:
                        pe.wait_ge(emptied[g % RING], g // RING)
                for n, k in enumerate(GROUPS[g]):
                    last = nc.tensor.transpose(ring[g % RING][:, n * ROWS:(n + 1) * ROWS], emb[:, k, :], ident[:, :])
                last.then_inc(filled, 1)

            def pick_table(i):
                pe.wait_ge(one_hot_ready, (i + 1) * PICK_CHUNKS)
                for n in range(PIECES):
                    pe.wait_ge(piece_ready[n], i + 1)
                if i >= 2:
                    pe.wait_ge(pick_out, i - 1)
                for c in range(PICK_CHUNKS):
                    for n in range(PIECES):
                        last = nc.tensor.matmul(ps_pick[i % 2][:, :], piece[n][:, i, c * DIM:(c + 1) * DIM],
                                                one_hot[i % 2][:, c, :], start=(c == 0 and n == 0),
                                                stop=(c == PICK_CHUNKS - 1 and n == PIECES - 1))
                last.then_inc(picked, 1)

            def pair_products(t):
                pe.wait_ge(fixed_placed, t + 1)
                for b in range(RING):
                    pe.wait_ge(emptied[b], bunch_use(t, b) // RING if isinstance(t, int)
                               else t * (USES // RING) + len(GROUPS) // RING)
                for i in range(BUNCHES):
                    if i >= RING:
                        pe.wait_ge(emptied[i % RING], t * (USES // RING) + (len(GROUPS) + i) // RING)
                    for n in range(BUNCH):
                        s = i * BUNCH + n
                        last = nc.tensor.matmul(ring[i % RING][0:PAIR_ROWS, n * PAIR_ROWS:(n + 1) * PAIR_ROWS],
                                                embT[:, s, 0:PAIR_ROWS], embT[:, s, 1:FEATS], start=True, stop=True)
                    last.then_inc(filled, 1)

            def h1_out(n):
                return ps_h1[n // 2][:, (n % 2) * ROWS:(n % 2 + 1) * ROWS]

            def layer1_dense(t):
                pe.wait_ge(fixed_placed, t + 1)
                for n in range(H1_TILES):
                    nc.tensor.matmul(h1_out(n), wd_sb[:, n * 128:(n + 1) * 128], embT[:, :, 0],
                                     start=(n % 2 == 0), stop=False, skip_group_check=True)

            def layer1_pairs(t):
                for b in range(RING):
                    pe.wait_ge(emptied[b], (t + 1) * (USES // RING))
                for n in range(H1_TILES):
                    for q in range(CHUNKS):
                        last = nc.tensor.matmul(h1_out(n), wp_sb[:, q, n * 128:(n + 1) * 128], z[:, q, :],
                                                start=False, stop=(q == CHUNKS - 1), skip_group_check=True)
                    if n % 2:
                        last.then_inc(h1_sum, 1)

            def layer2(t):
                for b in range(2):
                    pe.wait_ge(h1_ready[b], t + 1)
                for m in range(H2_TILES):
                    for k in range(H1_TILES):
                        last = nc.tensor.matmul(ps_h2[m][:, 0:ROWS], w2_sb[:, k, m * 128:(m + 1) * 128], h1[:, k, :],
                                                start=(k == 0), stop=(k == H1_TILES - 1))
                    last.then_inc(h2_sum, 1)

            def layer3(t):
                pe.wait_ge(h2_ready, (t + 1) * H2_TILES)
                for k in range(H2_TILES):
                    last = nc.tensor.matmul(ps_y, w3_sb[:, k:k + 1], h2[:, k, :],
                                            start=(k == 0), stop=(k == H2_TILES - 1))
                last.then_inc(y_sum, 1)

            pe.wait_ge(ident_ready, 1)
            pe.wait_ge(dense_in, 16)
            for t in range(TILES):
                last = nc.tensor.transpose(ps_dense[:, t * ROWS:(t + 1) * ROWS], dense_sb[:, t, :], ident[:, :])
            last.then_inc(dense_turned, 1)

            for i in range(PICKS):
                pick_table(i)
                for g in GROUPS_AFTER_PICK[i]:
                    transpose_group(0, g)
            pe.wait_ge(wd_ready, 1)
            pe.wait_ge(wp_in, 16)
            pe.wait_ge(w2_in, 16)
            pe.wait_ge(small_in, 48)
            pe.wait_ge(dense_out, 1)
            layer1_dense(0)

            with pe.Fori(0, TILES - 1) as t:
                pair_products(t)
                for g in (0, 1):
                    transpose_group(t + 1, g)
                layer1_pairs(t)
                for g in (2, 3):
                    transpose_group(t + 1, g)
                layer2(t)
                for g in (4, 5):
                    transpose_group(t + 1, g)
                layer1_dense(t + 1)
                layer3(t)
                for g in (6, 7):
                    transpose_group(t + 1, g)
            pair_products(TILES - 1)
            layer1_pairs(TILES - 1)
            layer2(TILES - 1)
            layer3(TILES - 1)

        @block.vector
        def _(dve):
            dve.wait_ge(vocab_ready, 1)
            for i in range(PICKS):
                dve.wait_ge(pick_ids_in[i], 16)
                nc.vector.tensor_copy(pick_ids[:, i, :], pick_ids32[:, i, :]).then_inc(pick_ids_ready, 1)
                dve.wait_ge(pick_ids_ready, i + 1)
                if i >= 2:
                    dve.wait_ge(picked, i - 1)
                for c in range(PICK_CHUNKS):
                    nc.vector.tensor_scalar(one_hot[i % 2][:, c, :], pick_ids[:, i, :], vocab[:, c:c + 1], None,
                                            ALU.is_equal).then_inc(one_hot_ready, 1)
                dve.wait_ge(piece_ready[0], i + 1)
                nc.vector.tensor_tensor(rest[:, i, :], table[:, i, :], piece[0][:, i, :],
                                        ALU.subtract).then_inc(rest_ready, 1)
                dve.wait_ge(rest_ready, i + 1)
                dve.wait_ge(piece_ready[1], i + 1)
                nc.vector.tensor_tensor(piece[2][:, i, :], rest[:, i, :], piece[1][:, i, :],
                                        ALU.subtract).then_inc(piece_ready[2], 1)
                if i == 1:
                    nc.vector.memset(z[:, :, :], 0.0).then_inc(z_clear, 1)
                if i:
                    for g in GROUPS_AFTER_PICK[i - 1]:
                        if g % 2 == 0:
                            copy_group(dve, nc.vector.tensor_copy, 0, g)
            dve.wait_ge(wd_in, 16)
            nc.vector.tensor_tensor(wd_sb[:, :], wd_in2[:, 0, :], wd_in2[:, 1, :], ALU.add).then_inc(wd_ready, 1)
            for g in GROUPS_AFTER_PICK[PICKS - 1]:
                if g % 2 == 0:
                    copy_group(dve, nc.vector.tensor_copy, 0, g)
            dve.wait_ge(z_clear, 1)
            dve.wait_ge(small_in, 48)

            def activate_h1(t):
                dve.wait_ge(h1_sum, t * 2 + 1)
                for n in (0, 1):
                    last = nc.vector.tensor_scalar(h1[:, n, :], ps_h1[0][:, n * ROWS:(n + 1) * ROWS],
                                                   b1_sb[:, n:n + 1], 0.0, ALU.add, ALU.max)
                last.then_inc(h1_ready[0], 1)

            def activate_h2(t):
                dve.wait_ge(h2_sum, t * H2_TILES + 1)
                nc.vector.tensor_scalar(h2[:, 0, :], ps_h2[0][:, 0:ROWS], b2_sb[:, 0:1], 0.0,
                                        ALU.add, ALU.max).then_inc(h2_ready, 1)

            def keep_y(t):
                dve.wait_ge(y_sum, t + 1)
                to = y[:, bass.ds(t * ROWS, ROWS)]
                nc.vector.tensor_copy(to, ps_y).then_inc(y_ready, 1)

            with dve.Fori(0, TILES - 1) as t:
                for i in range(0, BUNCHES, 2):
                    copy_bunch(dve, nc.vector.tensor_copy, t, i)
                copy_group(dve, nc.vector.tensor_copy, t + 1, 0)
                activate_h1(t)
                copy_group(dve, nc.vector.tensor_copy, t + 1, 2)
                activate_h2(t)
                copy_group(dve, nc.vector.tensor_copy, t + 1, 4)
                keep_y(t)
                copy_group(dve, nc.vector.tensor_copy, t + 1, 6)
            for i in range(0, BUNCHES, 2):
                copy_bunch(dve, nc.vector.tensor_copy, TILES - 1, i)
            activate_h1(TILES - 1)
            activate_h2(TILES - 1)
            keep_y(TILES - 1)

        @block.scalar
        def _(act):
            act.dma_start(table[:, 0, :], tables[PICKED[0]].rearrange("(p c) d -> p (c d)", c=PICK_CHUNKS)
                          ).then_inc(table_in[0], 16)

            def copy_pick(i):
                act.wait_ge(picked, i + 1)
                nc.scalar.copy(fixedT[:, 1 + i, :], ps_pick[i % 2][:, :]).then_inc(pick_out, 1)

            def place_fixed(t):
                nc.scalar.copy(embT[:, :, 0:FIXED],
                               fixedT[:, :, bass.ds(t * ROWS, ROWS)].rearrange("p f s -> p s f")
                               ).then_inc(fixed_placed, 1)

            for i in range(PICKS):
                act.wait_ge(table_in[i], 16)
                nc.scalar.copy(piece[0][:, i, :], table[:, i, :]).then_inc(piece_ready[0], 1)
                if i == 1:
                    act.wait_ge(dense_turned, 1)
                    nc.scalar.copy(fixedT[:, 0, :], ps_dense[:, :]).then_inc(dense_out, 1)
                act.wait_ge(rest_ready, i + 1)
                nc.scalar.copy(piece[1][:, i, :], rest[:, i, :]).then_inc(piece_ready[1], 1)
                if i >= 1:
                    copy_pick(i - 1)
                    for g in GROUPS_AFTER_PICK[i - 1]:
                        if g % 2:
                            copy_group(act, nc.scalar.copy, 0, g)
            copy_pick(PICKS - 1)
            act.wait_ge(pick_out, PICKS)
            act.wait_ge(dense_out, 1)
            place_fixed(0)
            for g in GROUPS_AFTER_PICK[PICKS - 1]:
                if g % 2:
                    copy_group(act, nc.scalar.copy, 0, g)
            act.wait_ge(z_clear, 1)
            act.wait_ge(small_in, 48)

            def activate_h1(t):
                act.wait_ge(h1_sum, t * 2 + 2)
                for n in (2, 3):
                    last = nc.scalar.activation(h1[:, n, :], ps_h1[1][:, (n - 2) * ROWS:(n - 1) * ROWS],
                                                ACT.Relu, bias=b1_sb[:, n:n + 1])
                last.then_inc(h1_ready[1], 1)

            def activate_h2(t):
                act.wait_ge(h2_sum, t * H2_TILES + 2)
                nc.scalar.activation(h2[:, 1, :], ps_h2[1][:, 0:ROWS], ACT.Relu,
                                     bias=b2_sb[:, 1:2]).then_inc(h2_ready, 1)

            with act.Fori(0, TILES - 1) as t:
                for i in range(1, BUNCHES, 2):
                    copy_bunch(act, nc.scalar.copy, t, i)
                act.wait_ge(filled, group_use(t + 1, 0) + 1)
                place_fixed(t + 1)
                copy_group(act, nc.scalar.copy, t + 1, 1)
                activate_h1(t)
                copy_group(act, nc.scalar.copy, t + 1, 3)
                activate_h2(t)
                copy_group(act, nc.scalar.copy, t + 1, 5)
                copy_group(act, nc.scalar.copy, t + 1, 7)
            for i in range(1, BUNCHES, 2):
                copy_bunch(act, nc.scalar.copy, TILES - 1, i)
            activate_h1(TILES - 1)
            activate_h2(TILES - 1)


def lay_out(inputs):
    import numpy as np
    arrays = {"dense": inputs["r_dense_features"], "ids": inputs["ids"]}
    arrays["ids_picked"] = np.asarray(inputs["ids"])[:, PICKED].T
    for i in range(TABLES):
        arrays[f"tbl_{i}"] = inputs[f"tbl_{i}"]
    w1 = np.asarray(inputs["W_top1"])
    arrays["w_dense"] = np.stack([w1[:DIM], w1[DIM + PAIRS:]], axis=1)
    w_pairs = np.zeros((128, CHUNKS, HID1), w1.dtype)
    row = DIM
    for a in range(FEATS):
        for b in range(a + 1, FEATS):
            f, g = sorted((SLOTS.index(a), SLOTS.index(b)))
            q, j = divmod(g - 1, QUADS)
            w_pairs[QUAD * j + f, q] = w1[row]
            row += 1
    arrays["w_pairs"] = w_pairs
    arrays["b1"] = np.asarray(inputs["b_top1"]).reshape(H1_TILES, 128).T
    arrays["w2"] = inputs["W_top2"]
    arrays["b2"] = np.asarray(inputs["b_top2"]).reshape(H2_TILES, 128).T
    arrays["w3"] = np.asarray(inputs["W_top3"]).reshape(H2_TILES, 128).T
    return {name: np.ascontiguousarray(a) for name, a in arrays.items()}


def kernel(**inputs):
    import concourse.bacc as _bacc
    from concourse import mybir as _mybir
    from concourse.bass_utils import run_bass_kernel_spmd as _run

    nc = _bacc.Bacc("TRN2", target_bir_lowering=False, num_devices=1)
    arrays = lay_out(inputs)
    ap = {name: nc.dram_tensor(f"in_{name}", a.shape, _mybir.dt.from_np(a.dtype), kind="ExternalInput").ap()
          for name, a in arrays.items()}
    out = nc.dram_tensor("out_y", (BATCH, 1), _mybir.dt.float32, kind="ExternalOutput").ap()
    dlrm_tower(nc, ap["dense"], ap["ids"], ap["ids_picked"], [ap[f"tbl_{i}"] for i in range(TABLES)], ap["w_dense"], ap["w_pairs"],
               ap["b1"], ap["w2"], ap["b2"], ap["w3"], out)
    r = _run(nc, [{f"in_{name}": a for name, a in arrays.items()}], core_ids=[0])
    return r.results[0]["out_y"]
```

```python
import concourse.bass as bass
from concourse import mybir
from contextlib import ExitStack

BATCH = 512
DIM = 128
TABLES = 26
FEATS = TABLES + 1
ROWS = 128
TILES = BATCH // ROWS
HID1, HID2 = 512, 256
PAIRS = FEATS * (FEATS - 1) // 2

PICKED = [8, 10, 11, 12, 16, 22, 23, 24]
PICKS = len(PICKED)
PICK_VOCAB = 1000
PICK_CHUNKS = 8
PICK_PARTS = PICK_VOCAB // PICK_CHUNKS
FIRST_CHUNKS = 4
FIRST, REST = slice(0, FIRST_CHUNKS * DIM), slice(FIRST_CHUNKS * DIM, PICK_CHUNKS * DIM)
DVE_CHUNKS = PICK_CHUNKS - 1
TABLE_BUFS = 3

GATHERED = [i for i in range(TABLES) if i not in PICKED]
FIXED = 1 + PICKS
SLOTS = [0] + [i + 1 for i in PICKED] + [i + 1 for i in GATHERED]

RING = 4
GROUP_SIZES = [4, 3, 3, 2, 2, 2, 1, 1]
GROUPS = [range(sum(GROUP_SIZES[:g]), sum(GROUP_SIZES[:g + 1])) for g in range(len(GROUP_SIZES))]
BUNCH = 16
BUNCHES = ROWS // BUNCH
USES = len(GROUPS) + BUNCHES
assert sum(GROUP_SIZES) == len(GATHERED) and USES % RING == 0 and len(GROUPS) % RING == 0

EARLY, LATE = range(0, RING), range(RING, len(GROUPS))
GROUPS_AFTER_PICK = [(), (0,), (1,), (2,), (3,), (4, 5), (6, 7), ()]
assert len(LATE) == RING and len(GROUPS_AFTER_PICK) == PICKS

SPAN = (FEATS - 1) // 2
ROUND_CHUNKS = 3
ROUND_COLS = FEATS // ROUND_CHUNKS
ROUND_ROWS = ROUND_COLS * SPAN
PITCH = FEATS + SPAN
assert FEATS % 2 and ROUND_CHUNKS * ROUND_COLS == FEATS
STAGE_PARTS = [(0, FEATS, 0, FEATS - 1, 0), (0, SPAN, SPAN + 1, FEATS, FEATS)]
TRIO = 3
TRIO_PAIRS = [(f, g) for g in range(TRIO) for f in range(g)]
QUADS, QUAD = 4, 32
PAIR_ROWS = FEATS - 1
QUAD_CHUNKS = (FEATS - TRIO) // QUADS
assert QUADS * QUAD_CHUNKS == FEATS - TRIO and PAIR_ROWS + len(TRIO_PAIRS) <= QUAD

H1_TILES = HID1 // 128
H2_TILES = HID2 // 128


def dlrm_tower(nc, dense_t, ids, ids_picked, tables, w_dense, w_round, w_quad, b1, w2, b2, w3, pairs_dram, out):
    fp32 = mybir.dt.float32
    fp32r = mybir.dt.float32r
    i32 = mybir.dt.int32
    ALU = mybir.AluOpType
    ACT = mybir.ActivationFunctionType

    ctx = ExitStack()
    with ctx:
        def sb(name, shape, dt=fp32):
            return ctx.enter_context(nc.sbuf_tensor(name, shape, dt))

        def bank(name):
            return ctx.enter_context(nc.psum_tensor(name, [128, 512], fp32))

        def sem(name):
            return ctx.enter_context(nc.semaphore(name))

        idx = sb("idx", [ROWS, TILES, TABLES], i32)
        emb = sb("emb", [ROWS, 2, len(GATHERED), DIM])
        fixedT = sb("fixedT", [DIM, FIXED, BATCH])
        embT = sb("embT", [DIM, ROWS, FEATS])
        pick_ids = sb("pick_ids", [PICK_PARTS, PICKS, BATCH], i32)
        vocab = sb("vocab", [PICK_PARTS, PICK_CHUNKS])
        minus_last = sb("minus_last", [PICK_PARTS, 1])
        distance = sb("distance", [PICK_PARTS, BATCH])
        one_hot = [sb(f"one_hot{b}", [PICK_PARTS, PICK_CHUNKS, BATCH], fp32r) for b in range(2)]
        table = sb("table", [PICK_PARTS, TABLE_BUFS, PICK_CHUNKS * DIM])
        high = [sb(f"high{b}", [PICK_PARTS, PICK_CHUNKS * DIM], fp32r) for b in range(2)]
        low = [sb(f"low{b}", [PICK_PARTS, PICK_CHUNKS * DIM], fp32r) for b in range(2)]
        stage = sb("stage", [FEATS, FEATS, ROWS])
        z_round = sb("z_round", [ROUND_ROWS, TILES - 1, ROUND_CHUNKS, ROWS])
        z_quad = sb("z_quad", [128, QUAD_CHUNKS, ROWS])
        trio_prod = sb("trio_prod", [DIM, len(TRIO_PAIRS), ROWS])
        trio_ones = sb("trio_ones", [DIM, len(TRIO_PAIRS), len(TRIO_PAIRS)])
        trio = sb("trio", [len(TRIO_PAIRS), ROWS])
        h1 = sb("h1", [128, H1_TILES, ROWS])
        h2 = sb("h2", [128, H2_TILES, ROWS])
        y = sb("y", [1, BATCH])
        wd_both = sb("wd_both", [DIM, 2, HID1])
        wd_sb = sb("wd_sb", [DIM, HID1])
        w_round_sb = sb("w_round_sb", [ROUND_ROWS, ROUND_CHUNKS, HID1])
        w_quad_sb = sb("w_quad_sb", [128, QUAD_CHUNKS, HID1])
        w2_sb = sb("w2_sb", [128, H1_TILES, HID2])
        w3_sb = sb("w3_sb", [128, H2_TILES])
        b1_sb = sb("b1_sb", [128, H1_TILES])
        b2_sb = sb("b2_sb", [128, H2_TILES])
        ident = sb("ident", [128, 128])

        ring = [bank(f"ring{b}") for b in range(RING)]
        ps_h1 = [bank(f"ps_h1{b}") for b in range(2)]
        ps_h2 = [bank(f"ps_h2{m}") for m in range(H2_TILES)]
        ps_y = ps_h2[0][0:1, ROWS:2 * ROWS]
        ps_trio = ps_h2[1][0:len(TRIO_PAIRS), ROWS:2 * ROWS]
        ps_pick = ps_h2

        idx0_in = sem("idx0_in")
        idx_in = sem("idx_in")
        dense_in = sem("dense_in")
        pick_ids_in = [sem(f"pick_ids_in{i}") for i in range(PICKS)]
        table_in = [sem(f"table_in{i}") for i in range(PICKS)]
        gathered = [[sem(f"gathered{b}_{g}") for g in range(len(GROUPS))] for b in range(2)]
        first_in = sem("first_in")
        wd_in = sem("wd_in")
        w_round_in = sem("w_round_in")
        w_quad_in = sem("w_quad_in")
        w2_in = sem("w2_in")
        b1_in = sem("b1_in")
        b2_in = sem("b2_in")
        w3_in = sem("w3_in")
        ident_clear = sem("ident_clear")
        ident_ready = sem("ident_ready")
        vocab_ready = sem("vocab_ready")
        z_clear = sem("z_clear")
        distance_ready = sem("distance_ready")
        act_hot_ready = sem("act_hot_ready")
        first_high_ready = sem("first_high_ready")
        high_ready = sem("high_ready")
        low_ready = sem("low_ready")
        one_hot_ready = sem("one_hot_ready")
        picked = sem("picked")
        pick_out = sem("pick_out")
        pairs_out = sem("pairs_out")
        pairs_in = sem("pairs_in")
        first_placed = sem("first_placed")
        fixed_placed = sem("fixed_placed")
        filled = sem("filled")
        emptied = [sem(f"emptied{b}") for b in range(RING)]
        ones_clear = sem("ones_clear")
        trio_ready = sem("trio_ready")
        trio_sum = sem("trio_sum")
        trio_out = sem("trio_out")
        trio_in = sem("trio_in")
        wd_ready = sem("wd_ready")
        h1_sum = sem("h1_sum")
        h1_ready = [sem(f"h1_ready{b}") for b in range(2)]
        h2_sum = sem("h2_sum")
        h2_ready = [sem(f"h2_ready{k}") for k in range(H2_TILES)]
        y_sum = sem("y_sum")
        y_ready = sem("y_ready")
        out_done = sem("out_done")

        block = ctx.enter_context(nc.Block())

        def group_use(t, g):
            return t * USES + g

        def bunch_use(t, i):
            return t * USES + len(GROUPS) + i

        def copy_group(eng, copy, t, g):
            eng.wait_ge(filled, group_use(t, g) + 1)
            k = len(GROUPS[g])
            src = ring[g % RING][:, 0:k * ROWS].rearrange("p (f s) -> p s f", f=k)
            first = FIXED + GROUPS[g][0]
            copy(embT[:, :, first:first + k], src).then_inc(emptied[g % RING], 1)

        def stage_bunch(eng, copy, t, i):
            eng.wait_ge(filled, bunch_use(t, i) + 1)
            src = ring[i % RING][0:FEATS, 0:BUNCH * FEATS].rearrange("p (s g) -> p g s", g=FEATS)
            copy(stage[:, :, i * BUNCH:(i + 1) * BUNCH], src).then_inc(emptied[i % RING], 1)

        def place_bunch(eng, copy, i):
            eng.wait_ge(filled, bunch_use(TILES - 1, i) + 1)
            src = ring[i % RING][0:PAIR_ROWS, 0:BUNCH * FEATS].rearrange("p (s g) -> p g s", g=FEATS)
            for j in range(QUADS):
                cols = src[:, TRIO + j::QUADS, :]
                last = copy(z_quad[QUAD * j:QUAD * j + PAIR_ROWS, 0:cols.shape[1], i * BUNCH:(i + 1) * BUNCH], cols)
            last.then_inc(emptied[i % RING], 1)

        @block.sync
        def _(sp):
            ids_v = ids.rearrange("(t p) f -> p t f", p=ROWS)
            sp.dma_start(idx[:, 0, :], ids_v[:, 0, :]).then_inc(idx0_in, 16)
            sp.dma_start(fixedT[:, 0, :], dense_t).then_inc(dense_in, 16)
            for i in range(1, PICKS):
                if i >= 2:
                    sp.wait_ge(high_ready, i - 1)
                if i >= TABLE_BUFS:
                    sp.wait_ge(low_ready, i - TABLE_BUFS + 1)
                if i == 2:
                    sp.dma_start(idx[:, 1:TILES, :], ids_v[:, 1:TILES, :]).then_inc(idx_in, 16)
                    sp.dma_start(wd_both[:, :, :], w_dense).then_inc(wd_in, 16)
                sp.dma_start(pick_ids[:, i, :], ids_picked[i:i + 1, :].to_broadcast([PICK_PARTS, BATCH])
                             ).then_inc(pick_ids_in[i], 16)
                sp.dma_start(table[:, i % TABLE_BUFS, :],
                             tables[PICKED[i]].rearrange("(p c) d -> p (c d)", c=PICK_CHUNKS)
                             ).then_inc(table_in[i], 16)
            sp.wait_ge(high_ready, PICKS - 1)
            sp.dma_start(b1_sb[:, :], b1).then_inc(b1_in, 16)
            sp.dma_start(b2_sb[:, :], b2).then_inc(b2_in, 16)
            sp.dma_start(w3_sb[:, :], w3).then_inc(w3_in, 16)
            sp.dma_start(w_round_sb[:, :, :], w_round).then_inc(w_round_in, 16)
            sp.dma_start(w2_sb[:, :, :], w2.rearrange("(k p) n -> p k n", p=128)).then_inc(w2_in, 16)

            def turn_pairs(t):
                for b in range(RING):
                    sp.wait_ge(emptied[b], (t + 1) * (USES // RING))
                for f, f_end, g, g_end, row in STAGE_PARTS:
                    to = pairs_dram[t, 0:FEATS * PITCH, :].rearrange("(g f) s -> f g s", f=PITCH)
                    sp.dma_start(to[row:row + f_end - f, g:g_end, :], stage[f:f_end, g:g_end, :]
                                 ).then_inc(pairs_out, 16)
                sp.wait_ge(pairs_out, (t + 1) * (16 * len(STAGE_PARTS)))
                turned = pairs_dram[t, :, :].rearrange("(g r) s -> g r s", r=PITCH + 1)
                if t:
                    sp.wait_ge(pairs_in, t * (16 * ROUND_CHUNKS))
                for c in range(ROUND_CHUNKS):
                    sp.dma_start(z_round[:, t, c, :], turned[c * ROUND_COLS:(c + 1) * ROUND_COLS, 1:SPAN + 1, :]
                                 ).then_inc(pairs_in, 16)

            turn_pairs(0)
            sp.wait_ge(trio_out, 1)
            sp.wait_ge(z_clear, 1)
            sp.dma_start(z_quad[PAIR_ROWS:PAIR_ROWS + len(TRIO_PAIRS), 0, :], trio[:, :]).then_inc(trio_in, 16)
            sp.dma_start(w_quad_sb[:, :, :], w_quad).then_inc(w_quad_in, 16)
            for t in range(1, TILES - 1):
                turn_pairs(t)
            sp.wait_ge(y_ready, TILES)
            sp.dma_start(out.rearrange("b o -> o b"), y[:, :]).then_inc(out_done, 16)
            sp.wait_ge(out_done, 16)

        @block.gpsimd
        def _(pool):
            nc.gpsimd.memset(ident[:, :], 0.0).then_inc(ident_clear, 1)
            nc.gpsimd.iota(vocab[:, :], [[1, PICK_CHUNKS]], base=0, channel_multiplier=PICK_CHUNKS,
                           allow_small_or_imprecise_dtypes=True).then_inc(vocab_ready, 1)
            nc.gpsimd.iota(minus_last[:, :], [[0, 1]], base=1 - PICK_CHUNKS, channel_multiplier=-PICK_CHUNKS,
                           allow_small_or_imprecise_dtypes=True).then_inc(vocab_ready, 1)
            pool.wait_ge(ident_clear, 1)
            nc.gpsimd.affine_select(out=ident[:, :], in_=ident[:, :], compare_op=ALU.not_equal, fill=1.0,
                                    base=0, pattern=[[-1, 128]], channel_multiplier=1).then_inc(ident_ready, 1)
            nc.gpsimd.memset(z_quad[:, :, :], 0.0).then_inc(z_clear, 1)
            pool.wait_ge(idx0_in, 16)
            for t in range(TILES):
                if t == 1:
                    pool.wait_ge(idx_in, 16)
                for g, feats in enumerate(GROUPS):
                    if t >= 2:
                        pool.wait_ge(filled, group_use(t - 2, g) + 1)
                    for k in feats:
                        i = GATHERED[k]
                        pool.indirect_dma_start(emb[:, t % 2, k, :], None, tables[i],
                                                bass.IndirectOffsetOnAxis(idx[:, t, i:i + 1], 0)
                                                ).then_inc(gathered[t % 2][g], 16)

        @block.tensor
        def _(pe):
            def transpose_group(t, g):
                pe.wait_ge(gathered[t % 2][g], (t // 2 + 1) * (16 * len(GROUPS[g])))
                if t or g >= RING:
                    pe.wait_ge(emptied[g % RING], group_use(t, g) // RING)
                for n, k in enumerate(GROUPS[g]):
                    last = nc.tensor.transpose(ring[g % RING][:, n * ROWS:(n + 1) * ROWS], emb[:, t % 2, k, :],
                                               ident[:, :])
                last.then_inc(filled, 1)

            def pick_table(i):
                if i:
                    pe.wait_ge(high_ready, i + 1)
                else:
                    pe.wait_ge(first_high_ready, 1)
                if i >= 2:
                    pe.wait_ge(pick_out, i - 1)
                for n, part in enumerate((high[i % 2], low[i % 2])):
                    if n:
                        pe.wait_ge(low_ready, i + 1)
                    for c in range(PICK_CHUNKS):
                        if i == 0 and n == 0 and c == FIRST_CHUNKS:
                            pe.wait_ge(high_ready, 1)
                        if n == 0:
                            if c < DVE_CHUNKS:
                                pe.wait_ge(one_hot_ready, i * DVE_CHUNKS + c + 1)
                            else:
                                pe.wait_ge(act_hot_ready, i + 1)
                        last = nc.tensor.matmul(ps_pick[i % 2][:, :], part[:, c * DIM:(c + 1) * DIM],
                                                one_hot[i % 2][:, c, :], start=(c == 0 and n == 0),
                                                stop=(c == PICK_CHUNKS - 1 and n == 1))
                last.then_inc(picked, 1)

            def pair_products(t):
                pe.wait_ge(first_placed, 1)
                pe.wait_ge(fixed_placed, t + 1)
                for b in range(RING):
                    pe.wait_ge(emptied[b], bunch_use(t, b) // RING)
                for i in range(BUNCHES):
                    if i >= RING:
                        pe.wait_ge(emptied[i % RING], bunch_use(t, i) // RING)
                    for n in range(BUNCH):
                        s = i * BUNCH + n
                        last = nc.tensor.matmul(ring[i % RING][0:FEATS, n * FEATS:(n + 1) * FEATS],
                                                embT[:, s, :], embT[:, s, :], start=True, stop=True)
                    last.then_inc(filled, 1)

            def h1_out(n):
                return ps_h1[n // 2][:, (n % 2) * ROWS:(n % 2 + 1) * ROWS]

            def layer1_dense(t):
                pe.wait_ge(wd_ready, 1)
                for n in range(H1_TILES):
                    nc.tensor.matmul(h1_out(n), wd_sb[:, n * 128:(n + 1) * 128],
                                     fixedT[:, 0, t * ROWS:(t + 1) * ROWS],
                                     start=(n % 2 == 0), stop=False, skip_group_check=True)

            def layer1_pairs(t):
                pe.wait_ge(w_round_in, 16)
                pe.wait_ge(pairs_in, (t + 1) * (16 * ROUND_CHUNKS))
                for n in range(H1_TILES):
                    for c in range(ROUND_CHUNKS):
                        last = nc.tensor.matmul(h1_out(n), w_round_sb[:, c, n * 128:(n + 1) * 128],
                                                z_round[:, t, c, :], start=False,
                                                stop=(c == ROUND_CHUNKS - 1), skip_group_check=True)
                    if n % 2:
                        last.then_inc(h1_sum, 1)

            def trio_pairs():
                pe.wait_ge(trio_ready, len(TRIO_PAIRS) + 1)
                pe.wait_ge(pick_out, PICKS)
                for i in range(len(TRIO_PAIRS)):
                    last = nc.tensor.matmul(ps_trio, trio_ones[:, i, :], trio_prod[:, i, :],
                                            start=(i == 0), stop=(i == len(TRIO_PAIRS) - 1))
                last.then_inc(trio_sum, 1)

            def last_layer1_pairs():
                pe.wait_ge(trio_in, 16)
                pe.wait_ge(w_quad_in, 16)
                for b in range(RING):
                    pe.wait_ge(emptied[b], TILES * (USES // RING))
                for n in range(H1_TILES):
                    for q in range(QUAD_CHUNKS):
                        last = nc.tensor.matmul(h1_out(n), w_quad_sb[:, q, n * 128:(n + 1) * 128], z_quad[:, q, :],
                                                start=False, stop=(q == QUAD_CHUNKS - 1), skip_group_check=True)
                    if n % 2:
                        last.then_inc(h1_sum, 1)

            def layer2(t):
                pe.wait_ge(w2_in, 16)
                for b in range(2):
                    pe.wait_ge(h1_ready[b], t + 1)
                    for m in range(H2_TILES):
                        for k in (2 * b, 2 * b + 1):
                            last = nc.tensor.matmul(ps_h2[m][:, 0:ROWS], w2_sb[:, k, m * 128:(m + 1) * 128],
                                                    h1[:, k, :], start=(k == 0), stop=(k == H1_TILES - 1))
                        if b:
                            last.then_inc(h2_sum, 1)

            def layer3(t):
                pe.wait_ge(w3_in, 16)
                for k in range(H2_TILES):
                    pe.wait_ge(h2_ready[k], t + 1)
                    last = nc.tensor.matmul(ps_y, w3_sb[:, k:k + 1], h2[:, k, :],
                                            start=(k == 0), stop=(k == H2_TILES - 1))
                last.then_inc(y_sum, 1)

            def transposes(t, groups):
                for g in groups:
                    transpose_group(t, g)

            pe.wait_ge(ident_ready, 1)
            for i in range(PICKS):
                pick_table(i)
                transposes(0, GROUPS_AFTER_PICK[i])

            pair_products(0)
            transposes(1, EARLY)
            trio_pairs()
            transposes(1, LATE)
            layer1_dense(0)
            pair_products(1)
            transposes(2, EARLY[:1])
            layer1_pairs(0)
            transposes(2, EARLY[1:3])
            layer2(0)
            transposes(2, EARLY[3:])
            transposes(2, LATE)
            layer3(0)
            layer1_dense(1)
            pair_products(2)
            transposes(3, EARLY[:1])
            layer1_pairs(1)
            transposes(3, EARLY[1:2])
            layer2(1)
            layer1_dense(2)
            transposes(3, EARLY[2:3])
            layer3(1)
            transposes(3, EARLY[3:])
            layer1_pairs(2)
            transposes(3, LATE)
            layer2(2)
            pair_products(3)
            layer3(2)
            layer1_dense(3)
            last_layer1_pairs()
            layer2(3)
            layer3(3)

        @block.vector
        def _(dve):
            dve.wait_ge(vocab_ready, 1)
            for i in range(PICKS):
                dve.wait_ge(pick_ids_in[i], 16)
                if i >= 2:
                    dve.wait_ge(picked, i - 1)
                for c in range(DVE_CHUNKS):
                    nc.vector.tensor_scalar(one_hot[i % 2][:, c, :], pick_ids[:, i, :], vocab[:, c:c + 1], None,
                                            ALU.is_equal).then_inc(one_hot_ready, 1)
                if i == 0:
                    dve.wait_ge(first_high_ready, 1)
                dve.wait_ge(high_ready, i + 1)
                nc.vector.tensor_tensor(low[i % 2][:, :], table[:, i % TABLE_BUFS, :], high[i % 2][:, :].bitcast(fp32),
                                        ALU.subtract).then_inc(low_ready, 1)
            dve.wait_ge(wd_in, 16)
            nc.vector.tensor_tensor(wd_sb[:, :], wd_both[:, 0, :], wd_both[:, 1, :], ALU.add).then_inc(wd_ready, 1)
            nc.vector.memset(trio_ones[:, :, :], 0.0).then_inc(ones_clear, 1)
            dve.wait_ge(ones_clear, 1)
            nc.vector.memset(trio_ones[:, :, :].rearrange("p i j -> p (i j)")[:, ::len(TRIO_PAIRS) + 1], 1.0
                             ).then_inc(trio_ready, 1)
            dve.wait_ge(dense_in, 16)
            dve.wait_ge(pick_out, TRIO - 1)
            for i, (f, g) in enumerate(TRIO_PAIRS):
                last_tile = slice((TILES - 1) * ROWS, BATCH)
                nc.vector.tensor_tensor(trio_prod[:, i, :], fixedT[:, f, last_tile], fixedT[:, g, last_tile],
                                        ALU.mult).then_inc(trio_ready, 1)
            dve.wait_ge(b1_in, 16)
            dve.wait_ge(b2_in, 16)

            def activate_h1(t):
                dve.wait_ge(h1_sum, t * 2 + 1)
                for n in (0, 1):
                    last = nc.vector.tensor_scalar(h1[:, n, :], ps_h1[0][:, n * ROWS:(n + 1) * ROWS],
                                                   b1_sb[:, n:n + 1], 0.0, ALU.add, ALU.max)
                last.then_inc(h1_ready[0], 1)

            def activate_h2(t):
                dve.wait_ge(h2_sum, t * H2_TILES + 1)
                nc.vector.tensor_scalar(h2[:, 0, :], ps_h2[0][:, 0:ROWS], b2_sb[:, 0:1], 0.0,
                                        ALU.add, ALU.max).then_inc(h2_ready[0], 1)

            def keep_y(t):
                dve.wait_ge(y_sum, t + 1)
                nc.vector.tensor_copy(y[:, t * ROWS:(t + 1) * ROWS], ps_y).then_inc(y_ready, 1)

            def stage_bunches(t):
                if t:
                    dve.wait_ge(pairs_out, t * (16 * len(STAGE_PARTS)))
                for i in range(0, BUNCHES, 2):
                    stage_bunch(dve, nc.vector.tensor_copy, t, i)

            def place_bunches():
                dve.wait_ge(z_clear, 1)
                for i in range(0, BUNCHES, 2):
                    place_bunch(dve, nc.vector.tensor_copy, i)

            def groups(t, these):
                for g in these:
                    copy_group(dve, nc.vector.tensor_copy, t, g)

            stage_bunches(0)
            groups(1, EARLY[::2])
            groups(1, LATE[::2])
            stage_bunches(1)
            groups(2, EARLY[:1])
            activate_h1(0)
            groups(2, EARLY[2:3])
            activate_h2(0)
            groups(2, LATE[::2])
            keep_y(0)
            stage_bunches(2)
            groups(3, EARLY[:1])
            activate_h1(1)
            activate_h2(1)
            groups(3, EARLY[2:3])
            keep_y(1)
            activate_h1(2)
            groups(3, LATE[::2])
            activate_h2(2)
            place_bunches()
            keep_y(2)
            activate_h1(3)
            activate_h2(3)
            keep_y(3)

        @block.scalar
        def _(act):
            act.dma_start(pick_ids[:, 0, :], ids_picked[0:1, :].to_broadcast([PICK_PARTS, BATCH])
                          ).then_inc(pick_ids_in[0], 16)
            first_table = tables[PICKED[0]].rearrange("(p c) d -> p (c d)", c=PICK_CHUNKS)
            act.dma_start(table[:, 0, FIRST], first_table[:, FIRST]).then_inc(first_in, 16)
            act.dma_start(table[:, 0, REST], first_table[:, REST]).then_inc(table_in[0], 16)

            def copy_pick(i):
                act.wait_ge(picked, i + 1)
                nc.scalar.copy(fixedT[:, 1 + i, :], ps_pick[i % 2][:, :]).then_inc(pick_out, 1)

            for i in range(PICKS):
                if i == 0:
                    act.wait_ge(first_in, 16)
                    nc.scalar.copy(high[0][:, FIRST], table[:, 0, FIRST]).then_inc(first_high_ready, 1)
                act.wait_ge(table_in[i], 16)
                if i >= 2:
                    act.wait_ge(picked, i - 1)
                part = slice(0, PICK_CHUNKS * DIM) if i else REST
                nc.scalar.copy(high[i % 2][:, part], table[:, i % TABLE_BUFS, part]).then_inc(high_ready, 1)
                act.wait_ge(pick_ids_in[i], 16)
                act.wait_ge(vocab_ready, 2)
                if i:
                    act.wait_ge(act_hot_ready, i)
                nc.scalar.activation(distance[:, :], pick_ids[:, i, :], ACT.Square,
                                     bias=minus_last[:, :]).then_inc(distance_ready, 1)
                act.wait_ge(distance_ready, i + 1)
                nc.scalar.activation(one_hot[i % 2][:, DVE_CHUNKS, :], distance[:, :], ACT.Relu, bias=1.0,
                                     scale=-1.0).then_inc(act_hot_ready, 1)
                if i >= 1:
                    copy_pick(i - 1)
                    for g in GROUPS_AFTER_PICK[i - 1]:
                        copy_group(act, nc.scalar.copy, 0, g)
            act.wait_ge(pick_out, PICKS - 1)
            act.wait_ge(dense_in, 16)
            nc.scalar.copy(embT[:, :, 0:PICKS], fixedT[:, 0:PICKS, 0:ROWS].rearrange("p f s -> p s f")
                           ).then_inc(first_placed, 1)
            act.wait_ge(picked, PICKS)
            nc.scalar.copy(embT[:, :, PICKS], ps_pick[(PICKS - 1) % 2][:, 0:ROWS]).then_inc(fixed_placed, 1)
            for g in GROUPS_AFTER_PICK[PICKS - 1]:
                copy_group(act, nc.scalar.copy, 0, g)
            copy_pick(PICKS - 1)
            act.wait_ge(pick_out, PICKS)
            act.wait_ge(b1_in, 16)
            act.wait_ge(b2_in, 16)

            def activate_h1(t):
                act.wait_ge(h1_sum, t * 2 + 2)
                for n in (2, 3):
                    last = nc.scalar.activation(h1[:, n, :], ps_h1[1][:, (n - 2) * ROWS:(n - 1) * ROWS],
                                                ACT.Relu, bias=b1_sb[:, n:n + 1])
                last.then_inc(h1_ready[1], 1)

            def activate_h2(t):
                act.wait_ge(h2_sum, t * H2_TILES + 2)
                nc.scalar.activation(h2[:, 1, :], ps_h2[1][:, 0:ROWS], ACT.Relu,
                                     bias=b2_sb[:, 1:2]).then_inc(h2_ready[1], 1)

            def stage_bunches(t):
                if t:
                    act.wait_ge(pairs_out, t * (16 * len(STAGE_PARTS)))
                for i in range(1, BUNCHES, 2):
                    stage_bunch(act, nc.scalar.copy, t, i)

            def place_bunches():
                act.wait_ge(z_clear, 1)
                for i in range(1, BUNCHES, 2):
                    place_bunch(act, nc.scalar.copy, i)

            def place_fixed(t):
                act.wait_ge(filled, group_use(t, 0) + 1)
                nc.scalar.copy(embT[:, :, 0:FIXED], fixedT[:, :, t * ROWS:(t + 1) * ROWS].rearrange("p f s -> p s f")
                               ).then_inc(fixed_placed, 1)

            def groups(t, these):
                for g in these:
                    copy_group(act, nc.scalar.copy, t, g)

            stage_bunches(0)
            place_fixed(1)
            groups(1, EARLY[1::2])
            act.wait_ge(trio_sum, 1)
            nc.scalar.copy(trio[:, :], ps_trio).then_inc(trio_out, 1)
            groups(1, LATE[1::2])
            stage_bunches(1)
            place_fixed(2)
            activate_h1(0)
            groups(2, EARLY[1:2])
            activate_h2(0)
            groups(2, EARLY[3:])
            groups(2, LATE[1::2])
            stage_bunches(2)
            place_fixed(3)
            activate_h1(1)
            groups(3, EARLY[1:2])
            activate_h2(1)
            groups(3, EARLY[3:])
            activate_h1(2)
            groups(3, LATE[1::2])
            activate_h2(2)
            place_bunches()
            activate_h1(3)
            activate_h2(3)


def lay_out(inputs):
    import numpy as np
    arrays = {"dense_t": np.asarray(inputs["r_dense_features"]).T, "ids": inputs["ids"]}
    arrays["ids_picked"] = np.asarray(inputs["ids"])[:, PICKED].T
    for i in range(TABLES):
        arrays[f"tbl_{i}"] = inputs[f"tbl_{i}"]
    w1 = np.asarray(inputs["W_top1"])
    arrays["w_dense"] = np.stack([w1[:DIM], w1[DIM + PAIRS:]], axis=1)
    w_round = np.zeros((ROUND_ROWS, ROUND_CHUNKS, HID1), w1.dtype)
    w_quad = np.zeros((128, QUAD_CHUNKS, HID1), w1.dtype)
    row = DIM
    for a in range(FEATS):
        for b in range(a + 1, FEATS):
            f, g = sorted((SLOTS.index(a), SLOTS.index(b)))
            if g < TRIO:
                w_quad[PAIR_ROWS + TRIO_PAIRS.index((f, g)), 0] = w1[row]
            else:
                q, j = divmod(g - TRIO, QUADS)
                w_quad[QUAD * j + f, q] = w1[row]
            d = g - f
            if d > SPAN:
                f, d = g, FEATS - d
            w_round[f % ROUND_COLS * SPAN + d - 1, f // ROUND_COLS] = w1[row]
            row += 1
    arrays["w_round"] = w_round
    arrays["w_quad"] = w_quad
    arrays["b1"] = np.asarray(inputs["b_top1"]).reshape(H1_TILES, 128).T
    arrays["w2"] = inputs["W_top2"]
    arrays["b2"] = np.asarray(inputs["b_top2"]).reshape(H2_TILES, 128).T
    arrays["w3"] = np.asarray(inputs["W_top3"]).reshape(H2_TILES, 128).T
    return {name: np.ascontiguousarray(a) for name, a in arrays.items()}


def kernel(**inputs):
    import concourse.bacc as _bacc
    from concourse import mybir as _mybir
    from concourse.bass_utils import run_bass_kernel_spmd as _run

    nc = _bacc.Bacc("TRN2", target_bir_lowering=False, num_devices=1)
    arrays = lay_out(inputs)
    ap = {name: nc.dram_tensor(f"in_{name}", a.shape, _mybir.dt.from_np(a.dtype), kind="ExternalInput").ap()
          for name, a in arrays.items()}
    out = nc.dram_tensor("out_y", (BATCH, 1), _mybir.dt.float32, kind="ExternalOutput").ap()
    pairs_dram = nc.dram_tensor("pairs_dram", (TILES - 1, FEATS * (PITCH + 1), ROWS), _mybir.dt.float32,
                                kind="Internal").ap()
    dlrm_tower(nc, ap["dense_t"], ap["ids"], ap["ids_picked"], [ap[f"tbl_{i}"] for i in range(TABLES)],
               ap["w_dense"], ap["w_round"], ap["w_quad"], ap["b1"], ap["w2"], ap["b2"], ap["w3"], pairs_dram, out)
    r = _run(nc, [{f"in_{name}": a for name, a in arrays.items()}], core_ids=[0])
    return r.results[0]["out_y"]
```
